# Optimizing a Trainium2 kernel written in Bass

```python
import numpy as np
import jax
import jax.numpy as jnp

def _softmax(x, axis=-1):
    return jax.nn.softmax(x, axis=axis)

def _gelu(x):
    return jax.nn.gelu(x, approximate=True)

def _silu(x):
    return jax.nn.silu(x)

def _sigmoid(x):
    return jax.nn.sigmoid(x)

def _layernorm(x, axis=-1, eps=1e-05):
    m = jnp.mean(x, axis=axis, keepdims=True)
    v = jnp.var(x, axis=axis, keepdims=True)
    return (x - m) / jnp.sqrt(v + eps)

def _scatter_add(tgt, idx, src, axis=0):
    return tgt.at[idx].add(src)

def _segment_sum(src, seg, n):
    return jax.ops.segment_sum(src, seg, n)
kernel_name = 'mk_conv_seq_d1_conv_nchw512_r2_243efe'

def setup_inputs(seed: int=0):
    np.random.seed(seed)
    _w = jnp.asarray

    def _rec_inputs():
        import jax
        import jax.numpy as jnp
        _gk = jax.random.key(seed)
        x = -9.26e-05 + 0.9999 * jax.random.normal(jax.random.fold_in(_gk, 1), (32, 256, 48, 48), jnp.float32)
        return x
    x = _rec_inputs()

    def _L0_conv_setup():
        import jax, jax.numpy as jnp
        import numpy as np
        G = 32
        EPS = 1e-05
        N_ITER = 10

        def isqrt_newton_schulz(A, num_iters):
            B, dim, _ = A.shape
            normA = jnp.linalg.norm(A.reshape(B, -1), axis=1)[:, None, None]
            Y = A / normA
            I = jnp.eye(dim, dtype=A.dtype)[None]
            Z = jnp.broadcast_to(I, A.shape)
            for _ in range(num_iters):
                T = 0.5 * (3.0 * I - Z @ Y)
                Y = Y @ T
                Z = T @ Z
            return Z / jnp.sqrt(normA)
        key = jax.random.key(seed)
        kx, kw, kb = jax.random.split(key, 3)
        x = jax.random.normal(kx, (32, 256, 48, 48), dtype=jnp.float32)
        weight1 = jnp.eye(G, dtype=jnp.float32)[None] + 0.01 * jax.random.normal(kw, (1, G, G), dtype=jnp.float32)
        bias1 = 0.01 * jax.random.normal(kb, (1, G, 1), dtype=jnp.float32)
        return {'x': x, 'weight1': weight1, 'bias1': bias1}
    _L0_conv_all = _L0_conv_setup()
    _L0_conv_in = {k: v for k, v in _L0_conv_all.items() if k in ('weight1', 'bias1')}
    del _L0_conv_all
    return {'x': x, 'L0_conv_weight1': _L0_conv_in['weight1'], 'L0_conv_bias1': _L0_conv_in['bias1']}

def reference(x, L0_conv_weight1, L0_conv_bias1):
    import jax
    import jax.numpy as jnp

    def _L0_conv_ref(x, weight1, bias1):
        import jax, jax.numpy as jnp
        import numpy as np
        G = 32
        EPS = 1e-05
        N_ITER = 10

        def isqrt_newton_schulz(A, num_iters):
            B, dim, _ = A.shape
            normA = jnp.linalg.norm(A.reshape(B, -1), axis=1)[:, None, None]
            Y = A / normA
            I = jnp.eye(dim, dtype=A.dtype)[None]
            Z = jnp.broadcast_to(I, A.shape)
            for _ in range(num_iters):
                T = 0.5 * (3.0 * I - Z @ Y)
                Y = Y @ T
                Z = T @ Z
            return Z / jnp.sqrt(normA)
        N, C, H, W = x.shape
        x1 = x.reshape(N, C // G, G, H, W).transpose(0, 2, 1, 3, 4).reshape(N, G, -1)
        mean = x1.mean(-1, keepdims=True)
        xc = x1 - mean
        M = xc.shape[2]
        cov = xc @ xc.transpose(0, 2, 1) / M + EPS * jnp.eye(G, dtype=x.dtype)
        decorr = isqrt_newton_schulz(cov, N_ITER)
        y = weight1 @ decorr @ xc + bias1
        return y.reshape(N, G, C // G, H, W).transpose(0, 2, 1, 3, 4).reshape(N, C, H, W)

    def _gn(v, G=32, eps=1e-05):
        B_, C_, H_, W_ = v.shape
        g = v.reshape(B_, G, C_ // G, H_, W_)
        m = jnp.mean(g, axis=(2, 3, 4), keepdims=True)
        s = jnp.var(g, axis=(2, 3, 4), keepdims=True)
        return ((g - m) / jnp.sqrt(s + eps)).reshape(v.shape)

    def _ln_c(v, eps=1e-06):
        m = jnp.mean(v, axis=1, keepdims=True)
        s = jnp.var(v, axis=1, keepdims=True)
        return (v - m) / jnp.sqrt(s + eps)

    def _ln_t(v, eps=1e-05):
        m = jnp.mean(v, axis=-1, keepdims=True)
        s = jnp.var(v, axis=-1, keepdims=True)
        return (v - m) / jnp.sqrt(s + eps)

    def _to_tokens(v):
        B_, C_, H_, W_ = v.shape
        return v.reshape(B_, C_, H_ * W_).transpose(0, 2, 1)

    def _from_tokens(t, like):
        B_, C_, H_, W_ = like.shape
        return t.transpose(0, 2, 1).reshape(B_, C_, H_, W_)
    x = _L0_conv_ref(x, L0_conv_weight1, L0_conv_bias1)
    return x

_drawn_inputs = setup_inputs


def setup_inputs(seed=0):
    import zlib

    import numpy as np

    out = dict(_drawn_inputs(seed))
    spreads = {}
    factors = {'L0_conv_bias1': 5.583}
    for name, (base, spread) in spreads.items():
        noise = np.random.default_rng([zlib.crc32(name.encode()), seed]).standard_normal(out[name].shape)
        drawn = base * np.exp(spread * noise) if base else spread * noise
        out[name] = jnp.asarray(drawn.astype(out[name].dtype))
    for name, factor in factors.items():
        out[name] = (out[name] * factor).astype(out[name].dtype)
    return out
```

```python
from contextlib import ExitStack

import concourse.bass as bass
from concourse import mybir

FP32 = mybir.dt.float32
ALU = mybir.AluOpType
ACT = mybir.ActivationFunctionType
AX = mybir.AxisListType

IMAGES, CHANNELS, PIXELS = 32, 256, 48 * 48
G = 32
P = 128
BLOCKS = P // G
HALVES = CHANNELS // P
SAMPLES = CHANNELS // G * PIXELS
EPS = 1e-5
NEWTON = 10
BATCH = BLOCKS
BATCHES = IMAGES // BATCH
SLOTS = 2 * BATCH
SHIFT_PIXELS = PIXELS // 2
COV_BLOCKS = PIXELS // P
T_BUFS = 2 * HALVES
CHUNK = PIXELS // 3
CHUNKS = HALVES * 3
BANK = 512

GATHER, NORM, FIRST_NEWTON = 0, 1, 2
FOLD, SPREAD, OFFSET = FIRST_NEWTON + 2 * NEWTON, FIRST_NEWTON + 2 * NEWTON + 1, FIRST_NEWTON + 2 * NEWTON + 2
PE_STEPS = OFFSET + 1
DVE_OPS = [5, 8] + [1, 2] * NEWTON + [5, 2, 1]
DVE_TOTAL = sum(DVE_OPS)
C_COV, C_OUTER, C_NORM, C_PRODUCT, C_NEXT, C_SPREAD, C_OFFSET = 0, 34, 66, 128, 192, 256, 400


def dve_after(step):
    return sum(DVE_OPS[:step + 1])


def whiten(nc, x, weight, bias, out):
    x_v = x.rearrange("n (h p) a b -> n p h (a b)", h=HALVES)
    out_v = out.rearrange("n (h p) a b -> n p h (a b)", h=HALVES)
    ctx = ExitStack()
    with ctx:
        def sb(name, shape, dt=FP32):
            return ctx.enter_context(nc.sbuf_tensor(name, shape, dt))

        def pb(name, shape):
            return ctx.enter_context(nc.psum_tensor(name, shape, FP32))

        def sem(name):
            return ctx.enter_context(nc.semaphore(name))

        xs = [sb(f"image{i}", [P, HALVES, PIXELS]) for i in range(SLOTS)]
        xt = [sb(f"transposed{i}", [P, PIXELS]) for i in range(T_BUFS)]
        junk = sb("junk", [P, SHIFT_PIXELS], mybir.dt.bfloat16)
        eye = sb("eye", [P, P])
        eye_col = sb("eye_col", [P, G])
        mean_col = sb("mean_col", [P, G])
        shift_mat = sb("shift_mat", [P, P])
        blocks = sb("blocks", [P, BLOCKS, G])
        pick = sb("pick", [P, BATCH, BLOCKS, G])
        eps_eye = sb("eps_eye", [P, G])
        eye15 = sb("eye15", [P, 2, G])
        w_nat = sb("w_nat", [P, G])
        w_t = sb("w_t", [P, G])
        b_col = sb("b_col", [P, 1])
        shift_sum = sb("shift_sum", [P, 2])
        shift = sb("shift", [P, 2])
        masked = sb("masked", [P, BLOCKS, G])
        stats = sb("stats", [P, 2, BATCH, G + HALVES])
        gathered = sb("gathered", [P, C_NORM])
        d_col = sb("d_col", [P, 1])
        neg_cov = sb("neg_cov", [P, G])
        cov = sb("cov", [P, G])
        cov_sq = sb("cov_sq", [P, G])
        col = sb("col", [P, 12])
        yz = sb("yz", [P, 2, G])
        yz_diag = sb("yz_diag", [P, 2, BLOCKS, G])
        tu = sb("tu", [P, 2, G])
        folded = sb("folded", [P, G + 1])
        apply_w = sb("apply_w", [P, BATCH, BLOCKS, G])
        d_rep = sb("d_rep", [P, BATCH])
        y_bias = sb("y_bias", [P, BATCH])
        credits = sb("credits", [P, 11])
        ROW, N2, ROOT, RECIP, TWICE, HALF_RN, RN, ROOT2, RECIP2, TWICE2, RSQ = (col[:, i:i + 1] for i in range(11))

        cov_ps = pb("cov_ps", [P, 2, BANK])
        y_ps = pb("y_ps", [P, 2, 2 * BANK])
        chain_ps = pb("chain_ps", [P, BANK])
        shift_ps = pb("shift_ps", [P, BANK])

        consts_in = sem("consts_in")
        loaded = [sem(f"loaded{i}") for i in range(SLOTS)]
        stored = [[sem(f"stored{i}_{h}") for h in range(HALVES)] for i in range(SLOTS)]
        eye_ready = sem("eye_ready")
        setup_pool = sem("setup_pool")
        setup_dve = sem("setup_dve")
        consts_ready = sem("consts_ready")
        summed = sem("summed")
        shift_ready = sem("shift_ready")
        shift_copied = sem("shift_copied")
        centred = sem("centred")
        transposed = sem("transposed")
        cov_done = sem("cov_done")
        cov_read = sem("cov_read")
        stats_ready = sem("stats_ready")
        chain_pe = sem("chain_pe")
        chain_dve = sem("chain_dve")
        chain_act = sem("chain_act")
        y_done = sem("y_done")
        y_read = sem("y_read")

        block = ctx.enter_context(nc.Block())

        def phases(eng, phase):
            phase(0, None, 0, 0, None)
            with eng.Fori(0, BATCHES // 2 - 1) as r:
                phase(2 * r + 1, 2 * r, 1, r, r)
                phase(2 * r + 2, 2 * r + 1, 0, r + 1, r)
            last = BATCHES // 2 - 1
            phase(BATCHES - 1, BATCHES - 2, 1, last, last)
            phase(None, BATCHES - 1, 0, None, last)


        @block.sync
        def _(sp):
            for b in range(BLOCKS):
                sp.dma_start(w_nat[G * b:G * (b + 1), :], weight[0]).then_inc(consts_in, 16)
                sp.dma_start(b_col[G * b:G * (b + 1), :], bias[0]).then_inc(consts_in, 16)
            for n in range(SLOTS):
                for h in range(HALVES):
                    sp.dma_start(xs[n][:, h, :], x_v[n, :, h, :]).then_inc(loaded[n], 16)
            with sp.Fori(0, BATCHES // 2 - 1) as r:
                for n in range(SLOTS):
                    for h in range(HALVES):
                        sp.wait_ge(stored[n][h], 16 * r + 16)
                        sp.dma_start(xs[n][:, h, :], x_v[bass.ds(SLOTS * r + SLOTS + n, 1), :, h, :].rearrange("o p s -> p (o s)")).then_inc(loaded[n], 16)

        @block.gpsimd
        def _(pool):
            nc.gpsimd.memset(eye[:], 0.0).then_inc(setup_pool, 1)
            pool.wait_ge(setup_pool, 1)
            nc.gpsimd.affine_select(out=eye[:], in_=eye[:], compare_op=ALU.not_equal, fill=1.0, base=0,
                                    pattern=[[-1, P]], channel_multiplier=1).then_inc(eye_ready, 1)

        @block.scalar
        def _(act):
            def centre(k, use, parity, i):
                n = BATCH * k + i
                slot = xs[BATCH * parity + i]
                act.wait_ge(loaded[BATCH * parity + i], 32 * use + 32)
                nc.scalar.activation(junk[:], slot[:, 0, 0:SHIFT_PIXELS], ACT.Identity,
                                     accum_out=shift_sum[:, i % 2:i % 2 + 1]).then_inc(summed, 1)
                act.wait_ge(shift_ready, n + 1)
                nc.scalar.copy(shift[:, i % 2:i % 2 + 1], shift_ps[:, 0:1]).then_inc(shift_copied, 1)
                act.wait_ge(shift_copied, n + 1 + 1)
                for h in range(HALVES):
                    ins = nc.scalar.activation(slot[:, h, :], slot[:, h, :], ACT.Identity,
                                               bias=shift[:, i % 2:i % 2 + 1],
                                               accum_out=stats[:, parity, i, G + h:G + h + 1])
                    ins.then_inc(centred, 1)

            def output(s, parity, i):
                n = BATCH * s + i
                slot = xs[BATCH * parity + i]
                for c in range(CHUNKS):
                    h, o = c // 3, c % 3 * CHUNK
                    if i == 0 and c == 0:
                        act.wait_ge(chain_dve, DVE_TOTAL * s + DVE_TOTAL)
                    act.wait_ge(y_done, CHUNKS * n + c + 1)
                    nc.scalar.activation(slot[:, h, o:o + CHUNK], y_ps[:, c % 2, 0:CHUNK], ACT.Identity,
                                         bias=y_bias[:, i:i + 1]).then_inc(y_read, 1)
                    if c % 3 == 2:
                        act.wait_ge(y_read, CHUNKS * n + c + 1 + 2)
                        act.dma_start(out_at(n, h), slot[:, h, :]).then_inc(stored[BATCH * parity + i][h], 16)

            def out_at(n, h):
                if isinstance(n, int):
                    return out_v[n, :, h, :]
                return out_v[bass.ds(n, 1), :, h, :].rearrange("o p s -> p (o s)")

            def phase(k, s, parity, k_use, s_use):
                if s is not None:
                    act.wait_ge(chain_dve, DVE_TOTAL * s + dve_after(GATHER) + 1)
                    nc.scalar.activation(ROOT, N2, ACT.Sqrt).then_inc(chain_act, 1)
                    act.wait_ge(chain_dve, DVE_TOTAL * s + dve_after(GATHER) + 5)
                    nc.scalar.activation(ROOT2, RN, ACT.Sqrt).then_inc(chain_act, 1)
                for i in range(BATCH):
                    if i >= 2 and s is not None:
                        output(s, 1 - parity, i - 2)
                        if i == 3:
                            output(s, 1 - parity, 2)
                    if k is not None and i + 1 < BATCH:
                        centre(k, k_use, parity, i + 1)
                    elif k is not None and not (isinstance(k, int) and k == BATCHES - 1):
                        centre(k + 1, k_use + parity, 1 - parity, 0)
                if s is not None:
                    output(s, 1 - parity, 3)

            centre(0, 0, 0, 0)
            phases(act, phase)
            for n in range(SLOTS):
                for h in range(HALVES):
                    act.wait_ge(stored[n][h], 16 * (IMAGES // SLOTS))

        @block.vector
        def _(dve):
            done = [0]

            def then(ins):
                done[0] += 1
                ins.then_inc(setup_dve, 1)
                dve.wait_ge(setup_dve, done[0])

            dve.wait_ge(eye_ready, 1)
            then(nc.vector.memset(blocks[:], 0.0))
            for b in range(BLOCKS):
                rows = slice(G * b, G * (b + 1))
                then(nc.vector.memset(blocks[rows, b, :], 1.0))
                then(nc.vector.tensor_copy(eye_col[rows, :], eye[rows, rows]))
            then(nc.vector.tensor_scalar(mean_col[:], eye_col[:], 1.0 / SAMPLES, None, ALU.mult))
            then(nc.vector.tensor_scalar(eps_eye[:], eye_col[:], EPS, None, ALU.mult))
            for b in range(BLOCKS):
                then(nc.vector.tensor_scalar(shift_mat[:, G * b:G * (b + 1)], eye_col[:],
                                             -1.0 / (BLOCKS * SHIFT_PIXELS), None, ALU.mult))
                for i in range(BATCH):
                    then(nc.vector.tensor_copy(pick[:, i, b, :], eye[:, G * i:G * (i + 1)]))
            for m in range(2):
                then(nc.vector.tensor_scalar(eye15[:, m, :], eye_col[:], 1.5, None, ALU.mult))
            dve.wait_ge(consts_in, 16 * 2 * BLOCKS)
            then(nc.vector.transpose(w_t[:], w_nat[:]))
            ahead = [shift_copied, stats_ready] + [cov_read, y_read] * 2 + [cov_done] * T_BUFS
            for i, free in enumerate(ahead):
                nc.vector.memset(credits[:, i:i + 1], 0.0).then_inc(free, 1)
            nc.vector.memset(credits[:, len(ahead):len(ahead) + 1], 0.0).then_inc(consts_ready, 1)

            def transpose(k, parity, i, h):
                m = HALVES * (BATCH * k + i) + h
                dve.wait_ge(centred, m + 1)
                dve.wait_ge(cov_done, m + 1)
                nc.vector.transpose(xt[HALVES * (i % 2) + h][:], xs[BATCH * parity + i][:, h, :]).then_inc(transposed, 1)

            def covariance_out(k, parity, i):
                n = BATCH * k + i
                dve.wait_ge(cov_done, HALVES * n + HALVES + T_BUFS)
                dve.wait_ge(stats_ready, n + 1)
                nc.vector.tensor_tensor(masked[:], cov_ps[:, i % 2, 0:P].rearrange("p (b g) -> p b g", b=BLOCKS),
                                        blocks[:], ALU.mult).then_inc(cov_read, 1)
                dve.wait_ge(cov_read, n + 1 + 2)
                nc.vector.tensor_reduce(stats[:, parity, i, 0:G], masked[:].rearrange("p b g -> p g b"),
                                        AX.X, ALU.add).then_inc(stats_ready, 1)

            def diagonal(dst, src, n):
                return nc.vector.tensor_tensor(
                    dst, src.unsqueeze(2).to_broadcast([P, n, BLOCKS, G]),
                    blocks[:].unsqueeze(1).to_broadcast([P, n, BLOCKS, G]), ALU.mult)

            def chain(s, first, last):
                for t in range(first, last):
                    at = [dve_after(t - 1) if t else 0]
                    dve.wait_ge(chain_pe, PE_STEPS * s + t + 1)

                    def link(ins):
                        at[0] += 1
                        ins.then_inc(chain_dve, 1)
                        dve.wait_ge(chain_dve, DVE_TOTAL * s + at[0])

                    if t == GATHER:
                        link(nc.vector.tensor_copy(gathered[:], chain_ps[:, 0:C_NORM]))
                        link(nc.vector.tensor_tensor(d_col[:], gathered[:, G:G + 1], gathered[:, G + 1:G + 2], ALU.add))
                        link(nc.vector.scalar_tensor_tensor(out=neg_cov[:], in0=gathered[:, C_OUTER:C_OUTER + G],
                                                            scalar=d_col[:, 0:1], in1=gathered[:, 0:G],
                                                            op0=ALU.mult, op1=ALU.subtract))
                        link(nc.vector.scalar_tensor_tensor(out=cov[:], in0=neg_cov[:], scalar=-1.0, in1=eps_eye[:],
                                                            op0=ALU.mult, op1=ALU.add))
                        link(nc.vector.scalar_tensor_tensor(out=cov_sq[:], in0=cov[:], scalar=1.0, in1=cov[:],
                                                            op0=ALU.mult, op1=ALU.mult, accum_out=ROW))
                    elif t == NORM:
                        link(nc.vector.tensor_copy(N2, chain_ps[:, C_NORM:C_NORM + 1]))
                        dve.wait_ge(chain_act, 2 * s + 1)
                        link(nc.vector.reciprocal(RECIP, ROOT))
                        link(nc.vector.scalar_tensor_tensor(out=TWICE, in0=N2, scalar=RECIP, in1=ROOT,
                                                            op0=ALU.mult, op1=ALU.add))
                        link(nc.vector.reciprocal(HALF_RN, TWICE))
                        link(nc.vector.tensor_scalar(RN, HALF_RN, 2.0, None, ALU.mult))
                        link(nc.vector.tensor_scalar(yz[:, 0, :], cov[:], RN, None, ALU.mult))
                        link(nc.vector.tensor_copy(yz[:, 1, :], eye_col[:]))
                        link(diagonal(yz_diag[:], yz[:], 2))
                    elif t < FOLD and (t - FIRST_NEWTON) % 2 == 0:
                        link(nc.vector.scalar_tensor_tensor(
                            out=tu[:], in0=chain_ps[:, C_PRODUCT:C_PRODUCT + 2 * G].rearrange("p (m g) -> p m g", m=2),
                            scalar=-0.5, in1=eye15[:], op0=ALU.mult, op1=ALU.add))
                    elif t < FOLD:
                        new = chain_ps[:, C_NEXT:C_NEXT + 2 * G].rearrange("p (m g) -> p m g", m=2)
                        link(nc.vector.tensor_copy(yz[:], new))
                        link(diagonal(yz_diag[:], new, 2))
                    elif t == FOLD:
                        dve.wait_ge(chain_act, 2 * s + 2)
                        link(nc.vector.reciprocal(RECIP2, ROOT2))
                        link(nc.vector.scalar_tensor_tensor(out=TWICE2, in0=RN, scalar=RECIP2, in1=ROOT2,
                                                            op0=ALU.mult, op1=ALU.add))
                        link(nc.vector.tensor_scalar(RSQ, TWICE2, 0.5, None, ALU.mult))
                        link(nc.vector.tensor_scalar(folded[:, 0:G], chain_ps[:, C_PRODUCT:C_PRODUCT + G], RSQ, None, ALU.mult))
                        link(nc.vector.tensor_copy(folded[:, G:G + 1], d_col[:]))
                    elif t == SPREAD:
                        dve.wait_ge(y_read, BATCH * CHUNKS * s + 2)
                        new = chain_ps[:, C_SPREAD:C_SPREAD + BATCH * (G + 1)].rearrange("p (i g) -> p i g", i=BATCH)
                        link(diagonal(apply_w[:], new[:, :, 0:G], BATCH))
                        link(nc.vector.tensor_copy(d_rep[:].unsqueeze(2), new[:, :, G:G + 1]))
                    else:
                        link(nc.vector.tensor_scalar(y_bias[:], chain_ps[:, C_OFFSET:C_OFFSET + BATCH], -1.0,
                                                     b_col[:, 0:1], ALU.mult, ALU.add))

            def phase(k, s, parity, k_use, s_use):
                for i in range(BATCH):
                    step = 12 * i
                    chained = i < 2 and s is not None
                    if chained:
                        chain(s, step, step + 6)
                    for h in range(HALVES):
                        if k is not None and i + 1 < BATCH:
                            transpose(k, parity, i + 1, h)
                        elif k is not None and not (isinstance(k, int) and k == BATCHES - 1):
                            transpose(k + 1, 1 - parity, 0, h)
                        if chained:
                            chain(s, step + 6 + 3 * h, step + 9 + 3 * h)
                    if k is not None:
                        covariance_out(k, parity, i)
                    if i == 1 and s is not None:
                        chain(s, 24, PE_STEPS)

            for h in range(HALVES):
                transpose(0, 0, 0, h)
            phases(dve, phase)

        @block.tensor
        def _(pe):
            def shift_of(k, i):
                n = BATCH * k + i
                pe.wait_ge(summed, n + 1)
                pe.wait_ge(shift_copied, n + 1)
                nc.tensor.matmul(shift_ps[:, 0:1], shift_mat[:], shift_sum[:, i % 2:i % 2 + 1],
                                 start=True, stop=True).then_inc(shift_ready, 1)

            def chain(s, parity, t):
                if t == GATHER:
                    pe.wait_ge(stats_ready, BATCH * s + BATCH + 1)
                    for i in range(BATCH):
                        rows = slice(G * i, G * (i + 1))
                        mine = stats[:, parity, i, :]
                        nc.tensor.matmul(chain_ps[rows, C_COV:C_COV + G + HALVES], mean_col[:], mine, start=True, stop=True)
                        for h in range(HALVES):
                            ins = nc.tensor.matmul(chain_ps[rows, C_OUTER:C_OUTER + G],
                                                   mine[:, G + h:G + h + 1].to_broadcast([P, G]), mean_col[:],
                                                   start=h == 0, stop=h == HALVES - 1)
                    ins.then_inc(chain_pe, 1)
                    return
                pe.wait_ge(chain_dve, DVE_TOTAL * s + dve_after(t - 1))
                y_d, z_d = (yz_diag[:, m, :, :].rearrange("p b g -> p (b g)") for m in range(2))
                if t == NORM:
                    ins = nc.tensor.matmul(chain_ps[:, C_NORM:C_NORM + 1], blocks[:].rearrange("p b g -> p (b g)"),
                                           ROW, start=True, stop=True)
                elif t < FOLD and (t - FIRST_NEWTON) % 2 == 0:
                    nc.tensor.matmul(chain_ps[:, C_PRODUCT:C_PRODUCT + G], z_d, yz[:, 0, :], start=True, stop=True)
                    ins = nc.tensor.matmul(chain_ps[:, C_PRODUCT + G:C_PRODUCT + 2 * G], y_d, yz[:, 1, :], start=True, stop=True)
                elif t < FOLD:
                    nc.tensor.matmul(chain_ps[:, C_NEXT:C_NEXT + G], y_d, tu[:, 0, :], start=True, stop=True)
                    ins = nc.tensor.matmul(chain_ps[:, C_NEXT + G:C_NEXT + 2 * G], z_d, tu[:, 1, :], start=True, stop=True)
                elif t == FOLD:
                    ins = nc.tensor.matmul(chain_ps[:, C_PRODUCT:C_PRODUCT + G], z_d, w_t[:], start=True, stop=True)
                elif t == SPREAD:
                    for i in range(BATCH):
                        at = C_SPREAD + (G + 1) * i
                        ins = nc.tensor.matmul(chain_ps[:, at:at + G + 1], pick[:, i, :, :].rearrange("p b g -> p (b g)"),
                                               folded[:], start=True, stop=True)
                else:
                    for i in range(BATCH):
                        ins = nc.tensor.matmul(chain_ps[:, C_OFFSET + i:C_OFFSET + i + 1],
                                               apply_w[:, i, :, :].rearrange("p b g -> p (b g)"), d_rep[:, i:i + 1],
                                               start=True, stop=True)
                ins.then_inc(chain_pe, 1)

            def covariance(k, i, s, parity, next_image):
                if k is not None:
                    n = BATCH * k + i
                    pe.wait_ge(cov_read, n + 1)
                for b in range(HALVES * COV_BLOCKS):
                    h, c = b // COV_BLOCKS, b % COV_BLOCKS
                    if k is not None:
                        if c == 0:
                            pe.wait_ge(transposed, HALVES * n + h + 1)
                        tile = xt[HALVES * (i % 2) + h][:, P * c:P * (c + 1)]
                        ins = nc.tensor.matmul(cov_ps[:, i % 2, 0:P], tile, tile, start=b == 0,
                                               stop=b == HALVES * COV_BLOCKS - 1)
                        if c == COV_BLOCKS - 1:
                            ins.then_inc(cov_done, 1)
                    if s is not None and i < 2 and b % 3 == 2:
                        chain(s, 1 - parity, 12 * i + b // 3)
                    if b == 8 and next_image is not None:
                        shift_of(*next_image)

            def output(s, parity, i):
                n = BATCH * s + i
                if i == 0:
                    pe.wait_ge(chain_dve, DVE_TOTAL * s + DVE_TOTAL)
                w = apply_w[:, i, :, :].rearrange("p b g -> p (b g)")
                for c in range(CHUNKS):
                    pe.wait_ge(y_read, CHUNKS * n + c + 1)
                    h, o = c // 3, c % 3 * CHUNK
                    for a in range(0, CHUNK, BANK):
                        z = min(BANK, CHUNK - a)
                        ins = nc.tensor.matmul(y_ps[:, c % 2, a:a + z], w, xs[BATCH * parity + i][:, h, o + a:o + a + z],
                                               start=True, stop=True)
                    ins.then_inc(y_done, 1)

            def phase(k, s, parity, k_use, s_use):
                for i in range(BATCH):
                    if i >= 2 and s is not None:
                        output(s, 1 - parity, i - 2)
                        if i == 3:
                            output(s, 1 - parity, 2)
                    following = None
                    if k is not None and i + 1 < BATCH:
                        following = (k, i + 1)
                    elif k is not None and not (isinstance(k, int) and k == BATCHES - 1):
                        following = (k + 1, 0)
                    covariance(k, i, s, parity, following)
                    if i == 1 and s is not None:
                        for t in range(24, PE_STEPS):
                            chain(s, 1 - parity, t)
                if s is not None:
                    output(s, 1 - parity, 3)

            pe.wait_ge(consts_ready, 1)
            shift_of(0, 0)
            phases(pe, phase)


def kernel(x, L0_conv_weight1, L0_conv_bias1):
    import numpy as np
    import concourse.bacc as bacc
    from concourse.bass_utils import run_bass_kernel_spmd

    nc = bacc.Bacc("TRN2", target_bir_lowering=False, num_devices=1)
    arrays = {"x": np.ascontiguousarray(x), "weight1": np.ascontiguousarray(L0_conv_weight1),
              "bias1": np.ascontiguousarray(L0_conv_bias1)}
    ins = [nc.dram_tensor(name, a.shape, mybir.dt.from_np(a.dtype), kind="ExternalInput").ap()
           for name, a in arrays.items()]
    out = nc.dram_tensor("y", arrays["x"].shape, FP32, kind="ExternalOutput").ap()
    whiten(nc, *ins, out)
    return run_bass_kernel_spmd(nc, [arrays], core_ids=[0]).results[0]["y"]
```

```python
from contextlib import ExitStack

import concourse.bass as bass
from concourse import mybir

FP32 = mybir.dt.float32
FP32R = mybir.dt.float32r
ALU = mybir.AluOpType
ACT = mybir.ActivationFunctionType
AX = mybir.AxisListType

IMAGES, CHANNELS, PIXELS = 32, 256, 48 * 48
G = 32
P = 128
BLOCKS = P // G
HALVES = CHANNELS // P
SAMPLES = CHANNELS // G * PIXELS
EPS = 1e-5
NEWTON = 10
PAIR = 2
PAIRS = IMAGES // PAIR
SLOTS = 8
PERIOD = SLOTS // PAIR
Q = PAIR * G
SHIFT_PIXELS = PIXELS // 2
PIECES = 3
PIECE = PIXELS // PIECES
IMAGE_PIECES = HALVES * PIECES
PIECE_BLOCKS = PIECE // P
ACT_HIGH = (2, 4)
SHIFT_AT = 1
CENTRE_PARTS = 2
RESTS = HALVES * CENTRE_PARTS
PLAIN = 2
BANK = 512

GATHER, NORM, NEXT_0 = 0, 1, 2
FOLD = NEXT_0 + 1 + 2 * (NEWTON - 1)
SPREAD = FOLD + 1
STEPS = SPREAD + 1
ASIDE = NEXT_0 + 4
EXTRA = [int(ASIDE <= t < ASIDE + 4) for t in range(STEPS)]
DVE_OPS = [m + e for m, e in zip([4, 5] + [1] * (STEPS - 3) + [2], EXTRA)]
DVE_TOTAL = sum(DVE_OPS)
PLACES = [1, 2] + list(range(4, STEPS + 2))
FLAT = PAIR * IMAGE_PIECES
STEP_AT = {place: t for t, place in enumerate(PLACES)}
assert PLACES[-1] == 2 * FLAT


BULK = [["S5"], ["T"], ["T"], [("S", 0)], ["T", "T"], [("S", 1), "T"],
        ["T", "T"], ["T"], [("S", 3)], ["T", "T"], ["E"], ["T", "T"],
        ["S5"], ["T", "T"], [("S", 0)], ["T", "T"], [("S", 1)], ["T", "T"],
        ["T"], ["T"], [("S", 3)], ["T", "T"], ["E"], ["T", "T"]]


C_COV, C_REST, C_OUTER, C_NORM = 0, G, G + RESTS, 2 * G + RESTS
C_PRODUCT, C_NEXT, C_SPREAD, C_OFFSET = 0, 2 * Q, 2 * Q, 0


def dve_after(step):
    return sum(DVE_OPS[:step + 1])


def dve_needed(step):
    return dve_after(step - 1) - EXTRA[step - 1]


def whiten(nc, x, weight, bias, out):
    x_v = x.rearrange("n (h p) a b -> n p h (a b)", h=HALVES)
    out_v = out.rearrange("n (h p) a b -> n p h (a b)", h=HALVES)
    ctx = ExitStack()
    with ctx:
        def sb(name, shape, dt=FP32):
            return ctx.enter_context(nc.sbuf_tensor(name, shape, dt))

        def pb(name, shape):
            return ctx.enter_context(nc.psum_tensor(name, shape, FP32))

        def sem(name):
            return ctx.enter_context(nc.semaphore(name))

        xs = [sb(f"image{i}", [P, HALVES, PIXELS]) for i in range(SLOTS)]
        xt = [sb(f"transposed{i}", [P, PIECE]) for i in range(PIECES)]
        with ExitStack() as early:
            whole = [early.enter_context(nc.sbuf_tensor(f"whole{i}", [P, 2, PIECE], FP32)) for i in range(IMAGE_PIECES)]
        parts = [sb(f"parts{i}", [P, 2, PIECE], FP32R) for i in range(IMAGE_PIECES)]
        junk = sb("junk", [P, SHIFT_PIXELS], mybir.dt.bfloat16)
        eye = sb("eye", [P, P])
        eye_col = sb("eye_col", [P, G])
        mean_col = sb("mean_col", [P, G])
        shift_mat = sb("shift_mat", [P, P])
        blocks = sb("blocks", [P, BLOCKS, G])
        pick = sb("pick", [Q, PAIR, BLOCKS, G])
        eps_eye = sb("eps_eye", [Q, G])
        blocks2 = sb("blocks2", [Q, PAIR, G])
        eye15 = sb("eye15", [Q, 2, Q])
        w_nat = sb("w_nat", [P, G])
        w_t = sb("w_t", [P, G])
        b_col = sb("b_col", [P, 1])
        shift_sum = sb("shift_sum", [P, 2])
        shift = sb("shift", [P, 2])
        masked = sb("masked", [P, 2, BLOCKS, G])
        stats = sb("stats", [P, 2, PAIR, 2 * G + RESTS])
        d_col = sb("d_col", [Q, 1])
        d_mask = sb("d_mask", [Q, PAIR])
        outer = sb("outer", [Q, G])
        cov = sb("cov", [Q, G])
        cov_sq = sb("cov_sq", [Q, G])
        col_all = sb("col", [P, 11])
        yz_all = sb("yz", [P, 2, Q])
        tu_all = sb("tu", [P, 2, Q])
        col, yz, tu = col_all[0:Q, :], yz_all[0:Q], tu_all[0:Q]
        folded = sb("folded", [Q, BLOCKS, G])
        apply_w = sb("apply_w", [P, 2, PAIR, BLOCKS, G])
        y_bias = sb("y_bias", [P, 2, PAIR])
        credits = sb("credits", [P, 24])
        ROW, ROOT, RECIP, TWICE, HALF_RN, HALF_ROOT, RECIP2, QUOTIENT, RSQ = (col[:, i:i + 1] for i in range(9))

        cov_ps = pb("cov_ps", [P, 2, BANK])
        y_ps = pb("y_ps", [P, 2, 2 * BANK])
        chain_ps = pb("chain_ps", [P, BANK])
        shift_ps = pb("shift_ps", [P, BANK])

        consts_in = sem("consts_in")
        loaded = [[sem(f"loaded{i}_{h}") for h in range(HALVES)] for i in range(SLOTS)]
        stored = [[sem(f"stored{i}_{h}") for h in range(HALVES)] for i in range(SLOTS)]
        eye_ready = sem("eye_ready")
        setup_pool = sem("setup_pool")
        setup_dve = sem("setup_dve")
        shift_mat_ready = sem("shift_mat_ready")
        consts_ready = sem("consts_ready")
        summed = sem("summed")
        shift_ready = sem("shift_ready")
        shift_copied = sem("shift_copied")
        centred = sem("centred")
        transposed = sem("transposed")
        high_dve = sem("high_dve")
        high_act = sem("high_act")
        low_ready = sem("low_ready")
        cov_done = sem("cov_done")
        cov_read = sem("cov_read")
        stats_ready = sem("stats_ready")
        chain_pe = sem("chain_pe")
        chain_dve = sem("chain_dve")
        chain_act = sem("chain_act")
        y_done = sem("y_done")
        y_read = sem("y_read")

        block = ctx.enter_context(nc.Block())

        def exists(r, c):
            return not isinstance(r, int) or 0 <= c < PAIRS

        def image(r, c, i):
            return PAIR * PERIOD * r + PAIR * c + i

        def slot_of(c, i):
            return PAIR * (c % PERIOD) + i

        def later(c, i, d):
            return c + (i + d) // PAIR, (i + d) % PAIR

        def plain(r, c):
            return isinstance(r, int) and c < PLAIN

        def split_piece(r, c, i, q):
            return IMAGE_PIECES * (image(r, c, i) - PAIR * PLAIN) + q

        def high_of(r, c, i, q, writer):
            mine = [p for p in range(IMAGE_PIECES) if (p in ACT_HIGH) == (writer == "act")]
            return len(mine) * (image(r, c, i) - PAIR * PLAIN) + mine.index(q) + 1

        def places(r, c):
            for f in range(FLAT):
                for m in range(2):
                    if f == 0 and m == 0:
                        t, pair = STEP_AT[2 * FLAT], c - 2
                    else:
                        t, pair = STEP_AT.get(2 * f + m), c - 1
                    yield f, m, t if exists(r, pair) else None, pair

        def output_at(c, f):
            pair, flat = (c - 2, f - 1) if f else (c - 3, FLAT - 1)
            return pair, flat // IMAGE_PIECES, flat % IMAGE_PIECES

        def phases(eng, phase):
            steady = (PAIRS - 3) // PERIOD
            for c in range(3):
                phase(0, c)
            with eng.Fori(0, steady) as r:
                for c in range(3, 3 + PERIOD):
                    phase(r, c)
            for c in range(3 + PERIOD * steady, PAIRS + 3):
                phase(0, c)

        def by_piece(r, c, i):
            return isinstance(r, int) and (c, i) == (PAIRS - 1, PAIR - 1)

        @block.sync
        def _(sp):
            for n in range(SLOTS):
                for h in range(HALVES):
                    sp.dma_start(xs[n][:, h, :], x_v[n, :, h, :]).then_inc(loaded[n][h], 16)
                if n == PAIR - 1:
                    for b in range(BLOCKS):
                        sp.dma_start(w_nat[G * b:G * (b + 1), :], weight[0]).then_inc(consts_in, 16)
                        sp.dma_start(b_col[G * b:G * (b + 1), :], bias[0]).then_inc(consts_in, 16)
            with sp.Fori(0, IMAGES // SLOTS - 1) as r:
                for n in range(SLOTS):
                    for h in range(HALVES):
                        sp.wait_ge(stored[n][h], 16 * r + 16)
                        sp.dma_start(xs[n][:, h, :], x_v[bass.ds(SLOTS * r + SLOTS + n, 1), :, h, :].rearrange("o p s -> p (o s)")).then_inc(loaded[n][h], 16)

        @block.gpsimd
        def _(pool):
            nc.gpsimd.memset(eye[:], 0.0).then_inc(setup_pool, 1)
            pool.wait_ge(setup_pool, 1)
            nc.gpsimd.affine_select(out=eye[:], in_=eye[:], compare_op=ALU.not_equal, fill=1.0, base=0,
                                    pattern=[[-1, P]], channel_multiplier=1).then_inc(eye_ready, 1)

            with pool.Fori(0, IMAGES - PAIR * PLAIN) as n:
                highs = {True: 0, False: 0}
                for q in range(IMAGE_PIECES):
                    by_act = q in ACT_HIGH
                    highs[by_act] += 1
                    if by_act:
                        pool.wait_ge(high_act, len(ACT_HIGH) * n + highs[True])
                    else:
                        pool.wait_ge(high_dve, (IMAGE_PIECES - len(ACT_HIGH)) * n + highs[False])
                    nc.gpsimd.tensor_tensor(parts[q][:, 1, :], xt[q % PIECES][:], parts[q][:, 0, :].bitcast(FP32),
                                            ALU.subtract).then_inc(low_ready, 1)

        @block.scalar
        def _(act):
            def sum_shift(r, c, i):
                n = image(r, c, i)
                act.wait_ge(loaded[slot_of(c, i)][0], 16 * (r + c // PERIOD) + 16)
                nc.scalar.activation(junk[:], xs[slot_of(c, i)][:, 0, 0:SHIFT_PIXELS], ACT.Identity,
                                     accum_out=shift_sum[:, i:i + 1]).then_inc(summed, 1)

            def centre(r, c, i, k):
                n = image(r, c, i)
                h, o = k // CENTRE_PARTS, k % CENTRE_PARTS * (PIXELS // CENTRE_PARTS)
                if k == 0:
                    act.wait_ge(shift_ready, n + 1)
                    nc.scalar.copy(shift[:, i:i + 1], shift_ps[:, 0:1]).then_inc(shift_copied, 1)
                    act.wait_ge(shift_copied, n + 1 + 1)
                part = xs[slot_of(c, i)][:, h, o:o + PIXELS // CENTRE_PARTS]
                act.wait_ge(loaded[slot_of(c, i)][h], 16 * (r + c // PERIOD) + 16)
                nc.scalar.activation(part, part, ACT.Identity, bias=shift[:, i:i + 1],
                                     accum_out=stats[:, c % 2, i, 2 * G + k:2 * G + k + 1]).then_inc(centred, 1)

            def high(r, c, i, q):
                act.wait_ge(transposed, 2 * (IMAGE_PIECES * image(r, c, i) + q) + 2)
                act.wait_ge(cov_done, IMAGE_PIECES * image(r, c, i) + q + 1)
                nc.scalar.copy(parts[q][:, 0, :], xt[q % PIECES][:]).then_inc(high_act, 1)

            def output(r, c, i, q):
                m = IMAGE_PIECES * image(r, c, i) + q
                h, o = q // PIECES, q % PIECES * PIECE
                if i == 0 and q == 0:
                    act.wait_ge(chain_dve, DVE_TOTAL * (PERIOD * r + c) + DVE_TOTAL)
                act.wait_ge(y_done, m + 1)
                slot = xs[slot_of(c, i)]
                nc.scalar.activation(slot[:, h, o:o + PIECE], y_ps[:, q % 2, 0:PIECE], ACT.Identity,
                                     bias=y_bias[:, c % 2, i:i + 1]).then_inc(y_read, 1)
                if by_piece(r, c, i):
                    act.wait_ge(y_read, m + 1 + 2)
                    act.dma_start(out_v[image(r, c, i), :, h, o:o + PIECE], slot[:, h, o:o + PIECE]).then_inc(
                        stored[slot_of(c, i)][h], 16)
                elif q % PIECES == PIECES - 1:
                    act.wait_ge(y_read, m + 1 + 2)
                    n = image(r, c, i)
                    dst = out_v[n, :, h, :] if isinstance(n, int) else out_v[bass.ds(n, 1), :, h, :].rearrange("o p s -> p (o s)")
                    act.dma_start(dst, slot[:, h, :]).then_inc(stored[slot_of(c, i)][h], 16)

            def root(r, c, half):
                s = PERIOD * r + c
                if half:
                    act.wait_ge(chain_dve, DVE_TOTAL * s + dve_after(NORM))
                    nc.scalar.activation(HALF_ROOT, HALF_RN, ACT.Sqrt, scale=0.5).then_inc(chain_act, 1)
                else:
                    act.wait_ge(chain_pe, STEPS * s + NORM + 1)
                    nc.scalar.activation(ROOT, chain_ps[0:Q, C_NORM:C_NORM + 1], ACT.Sqrt).then_inc(chain_act, 1)

            def phase(r, c):
                for f in range(FLAT):
                    i, q = f // IMAGE_PIECES, f % IMAGE_PIECES
                    if f in (1, 2) and exists(r, c - 1):
                        root(r, c - 1, f == 2)
                    done = output_at(c, f)
                    if exists(r, done[0]):
                        output(r, *done)
                    following, ahead = later(c, i, 1), later(c, i, 2)
                    for p in ACT_HIGH:
                        if q == p + 1 and exists(r, following[0]) and not plain(r, following[0]):
                            high(r, *following, p)
                    if exists(r, ahead[0]):
                        if q == 0:
                            sum_shift(r, *ahead)
                        elif q <= RESTS:
                            centre(r, *ahead, q - 1)

            for i in range(PAIR):
                sum_shift(0, 0, i)
                for k in range(RESTS):
                    centre(0, 0, i, k)
            phases(act, phase)
            for n in range(SLOTS):
                for h in range(HALVES):
                    stores = IMAGES // SLOTS + (PIECES - 1 if n == SLOTS - 1 else 0)
                    act.wait_ge(stored[n][h], 16 * stores)

        @block.vector
        def _(dve):
            done = [0]

            def then(ins):
                done[0] += 1
                ins.then_inc(setup_dve, 1)
                dve.wait_ge(setup_dve, done[0])

            dve.wait_ge(eye_ready, 1)
            for b in range(BLOCKS):
                rows = slice(G * b, G * (b + 1))
                then(nc.vector.tensor_copy(eye_col[rows, :], eye[rows, rows]))
            for b in range(BLOCKS):
                then(nc.vector.tensor_scalar(shift_mat[:, G * b:G * (b + 1)], eye_col[:],
                                             -1.0 / (BLOCKS * SHIFT_PIXELS), None, ALU.mult))
            nc.vector.memset(credits[:, 0:1], 0.0).then_inc(shift_copied, 1)
            nc.vector.memset(credits[:, 1:2], 0.0).then_inc(shift_mat_ready, 1)
            for padded in (col_all, yz_all, blocks):
                then(nc.vector.memset(padded[:], 0.0))
            then(nc.vector.memset(tu_all[:], 0.0))
            for b in range(BLOCKS):
                then(nc.vector.memset(blocks[G * b:G * (b + 1), b, :], 1.0))
            then(nc.vector.tensor_scalar(mean_col[:], eye_col[:], 1.0 / SAMPLES, None, ALU.mult))
            then(nc.vector.tensor_scalar(eps_eye[:], eye_col[0:Q, :], EPS, None, ALU.mult))
            for b in range(BLOCKS):
                for i in range(PAIR):
                    then(nc.vector.tensor_copy(pick[:, i, b, :], eye[0:Q, G * i:G * (i + 1)]))
            then(nc.vector.tensor_scalar(blocks2[:], blocks[0:Q, 0:PAIR, :], 2.0, None, ALU.mult))
            for m in range(2):
                then(nc.vector.tensor_scalar(eye15[:, m, :], eye[0:Q, 0:Q], 1.5, None, ALU.mult))
            ahead = [stats_ready] + [cov_read, y_read] * 2 + [cov_done] * IMAGE_PIECES + [low_ready] * PIECES
            for i, free in enumerate(ahead):
                nc.vector.memset(credits[:, 2 + i:3 + i], 0.0).then_inc(free, 1)
            nc.vector.memset(credits[:, 2 + len(ahead):3 + len(ahead)], 0.0).then_inc(consts_ready, 1)

            def transpose(r, c, i, k):
                q, part = k // 2, k % 2
                h, o = q // PIECES, q % PIECES
                a = PIECE // 2 * part
                z = a + PIECE // 2
                of_half = PIECE * o + a
                if of_half % (PIXELS // CENTRE_PARTS) == 0:
                    dve.wait_ge(centred, RESTS * image(r, c, i) + CENTRE_PARTS * h + of_half // (PIXELS // CENTRE_PARTS) + 1)
                if plain(r, c):
                    if part == 0:
                        dve.wait_ge(cov_done, IMAGE_PIECES * image(r, c, i) + q + 1)
                    dst = whole[q][:, 0, a:z]
                else:
                    if part == 0:
                        dve.wait_ge(low_ready, split_piece(r, c, i, q) + 1)
                    dst = xt[o][:, a:z]
                nc.vector.transpose(dst, xs[slot_of(c, i)][:, h, of_half:of_half + PIECE // 2]).then_inc(transposed, 1)

            def high(r, c, i, q):
                m = IMAGE_PIECES * image(r, c, i) + q
                dve.wait_ge(transposed, 2 * m + 2)
                dve.wait_ge(cov_done, m + 1)
                nc.vector.tensor_copy(parts[q][:, 0, :], xt[q % PIECES][:]).then_inc(high_dve, 1)

            def covariance_out(r, c, i):
                n = image(r, c, i)
                dve.wait_ge(cov_done, IMAGE_PIECES * (n + 1) + IMAGE_PIECES)
                dve.wait_ge(stats_ready, n + 1)
                kinds = 1 if plain(r, c) else 2
                nc.vector.tensor_tensor(masked[:, 0:kinds],
                                        cov_ps[:, i, 0:kinds * P].rearrange("p (m b g) -> p m b g", m=kinds, b=BLOCKS),
                                        blocks[:].unsqueeze(1).to_broadcast([P, kinds, BLOCKS, G]), ALU.mult).then_inc(cov_read, 1)
                dve.wait_ge(cov_read, n + 1 + 2)
                nc.vector.tensor_reduce(stats[:, c % 2, i, 0:kinds * G].rearrange("p (m g) -> p m g", m=kinds),
                                        masked[:, 0:kinds].rearrange("p m b g -> p m g b"),
                                        AX.X, ALU.add).then_inc(stats_ready, 1)

            def diagonal(dst, src, n, rows, count):
                return nc.vector.tensor_tensor(
                    dst, src.unsqueeze(2).to_broadcast([rows, n, count, G]),
                    blocks[0:rows, 0:count, :].unsqueeze(1).to_broadcast([rows, n, count, G]), ALU.mult)

            def chain(r, c, t):
                s = PERIOD * r + c
                at = [dve_after(t - 1) if t else 0]
                dve.wait_ge(chain_pe, STEPS * s + t + 1)

                def link(ins):
                    at[0] += 1
                    ins.then_inc(chain_dve, 1)
                    dve.wait_ge(chain_dve, DVE_TOTAL * s + at[0])

                product = chain_ps[0:Q, C_PRODUCT:C_PRODUCT + 2 * Q].rearrange("p (m g) -> p m g", m=2)
                following = chain_ps[0:Q, C_NEXT:C_NEXT + 2 * Q].rearrange("p (m g) -> p m g", m=2)
                if t == GATHER:
                    link(nc.vector.tensor_reduce(d_col[:], chain_ps[0:Q, C_REST:C_REST + RESTS], AX.X, ALU.add))
                    link(nc.vector.scalar_tensor_tensor(out=outer[:], in0=chain_ps[0:Q, C_OUTER:C_OUTER + G],
                                                        scalar=d_col[:, 0:1], in1=eps_eye[:],
                                                        op0=ALU.mult, op1=ALU.subtract))
                    link(nc.vector.scalar_tensor_tensor(out=cov[:], in0=chain_ps[0:Q, C_COV:C_COV + G], scalar=1.0,
                                                        in1=outer[:], op0=ALU.mult, op1=ALU.subtract))
                    link(nc.vector.scalar_tensor_tensor(out=cov_sq[:], in0=cov[:], scalar=1.0, in1=cov[:],
                                                        op0=ALU.mult, op1=ALU.mult, accum_out=ROW))
                elif t == NORM:
                    dve.wait_ge(chain_act, 2 * s + 1)
                    link(nc.vector.reciprocal(RECIP, ROOT))
                    link(nc.vector.scalar_tensor_tensor(out=TWICE, in0=chain_ps[0:Q, C_NORM:C_NORM + 1], scalar=RECIP,
                                                        in1=ROOT, op0=ALU.mult, op1=ALU.add))
                    link(nc.vector.reciprocal(HALF_RN, TWICE))
                    link(nc.vector.scalar_tensor_tensor(
                        out=yz[:, 0, :].rearrange("p (b g) -> p b g", b=PAIR),
                        in0=cov[:].unsqueeze(1).to_broadcast([Q, PAIR, G]), scalar=HALF_RN, in1=blocks2[:],
                        op0=ALU.mult, op1=ALU.mult))
                    link(nc.vector.scalar_tensor_tensor(
                        out=yz[:, 1, :], in0=yz[:, 0, :], scalar=-0.5, in1=eye15[:, 0, :], op0=ALU.mult, op1=ALU.add))
                elif t == NEXT_0:
                    link(nc.vector.tensor_copy(yz[:, 0, :], following[:, 0, :]))
                elif t < FOLD and (t - NEXT_0) % 2 == 1:
                    first = 1 if t == FOLD - 2 else 0
                    link(nc.vector.scalar_tensor_tensor(out=tu[:, first:2], in0=product[:, first:2], scalar=-0.5,
                                                        in1=eye15[:, first:2], op0=ALU.mult, op1=ALU.add))
                elif t < FOLD:
                    first = 1 if t == FOLD - 1 else 0
                    link(nc.vector.tensor_copy(yz[:, first:2], following[:, first:2]))
                elif t == FOLD:
                    link(nc.vector.tensor_scalar(
                        folded[:], chain_ps[0:Q, C_PRODUCT:C_PRODUCT + G].unsqueeze(1).to_broadcast([Q, BLOCKS, G]),
                        RSQ, None, ALU.mult))
                else:
                    if exists(r, c - 2):
                        dve.wait_ge(y_read, IMAGE_PIECES * image(r, c - 1, 0) + 2)
                    spread = chain_ps[:, C_SPREAD:C_SPREAD + PAIR * G].rearrange("p (i g) -> p i g", i=PAIR)
                    link(diagonal(apply_w[:, c % 2], spread, PAIR, P, BLOCKS))
                    link(nc.vector.tensor_scalar(y_bias[:, c % 2, :], chain_ps[:, C_OFFSET:C_OFFSET + PAIR], -1.0,
                                                 b_col[:, 0:1], ALU.mult, ALU.add))

                if t == ASIDE:
                    link(nc.vector.tensor_scalar(d_mask[:], blocks[0:Q, 0:PAIR, 0], d_col[:, 0:1], None, ALU.mult))
                elif t == ASIDE + 1:
                    dve.wait_ge(chain_act, 2 * s + 2)
                    link(nc.vector.reciprocal(RECIP2, HALF_ROOT))
                elif t == ASIDE + 2:
                    link(nc.vector.tensor_scalar(QUOTIENT, RECIP2, HALF_RN, 0.5, ALU.mult, ALU.mult))
                elif t == ASIDE + 3:
                    link(nc.vector.tensor_tensor(RSQ, QUOTIENT, HALF_ROOT, ALU.add))

            def phase(r, c):
                halves_done = 0
                for f, m, t, pair in places(r, c):
                    i, q = f // IMAGE_PIECES, f % IMAGE_PIECES
                    if t is not None:
                        chain(r, pair, t)
                    if q == m == 0:
                        halves_done = 0
                    following = later(c, i, 1)
                    for work in BULK[2 * f + m]:
                        if work == "E":
                            if exists(r, c):
                                covariance_out(r, c, i)
                        elif work == "S5":
                            if exists(r, c) and not plain(r, c):
                                high(r, c, i, IMAGE_PIECES - 1)
                        elif exists(r, following[0]):
                            if work == "T":
                                transpose(r, *following, halves_done)
                                halves_done += 1
                            elif not plain(r, following[0]):
                                high(r, *following, work[1])

            for k in range(2 * IMAGE_PIECES):
                transpose(0, 0, 0, k)
            dve.wait_ge(consts_in, 16 * 2 * BLOCKS)
            then(nc.vector.transpose(w_t[:], w_nat[:]))
            phases(dve, phase)

        @block.tensor
        def _(pe):
            def shift_of(r, c, i):
                n = image(r, c, i)
                pe.wait_ge(summed, n + 1)
                pe.wait_ge(shift_copied, n + 1)
                nc.tensor.matmul(shift_ps[:, 0:1], shift_mat[:], shift_sum[:, i:i + 1],
                                 start=True, stop=True).then_inc(shift_ready, 1)

            def chain(r, c, t):
                s = PERIOD * r + c
                if t == GATHER:
                    pe.wait_ge(stats_ready, PAIR * s + PAIR + 1)
                    if exists(r, c - 1):
                        pe.wait_ge(chain_dve, DVE_TOTAL * s)
                    for i in range(PAIR):
                        rows = slice(G * i, G * (i + 1))
                        squares, crossed, rests = (stats[:, c % 2, i, G * m:min(G * (m + 1), 2 * G + RESTS)] for m in range(3))
                        sums = chain_ps[rows, C_COV:C_COV + G]
                        nc.tensor.matmul(sums, mean_col[:], squares, start=True, stop=plain(r, c))
                        if not plain(r, c):
                            nc.tensor.matmul(sums, mean_col[:], crossed, start=False, stop=False)
                            nc.tensor.matmul(sums, crossed, mean_col[:], start=False, stop=True)
                        nc.tensor.matmul(chain_ps[rows, C_REST:C_REST + RESTS], mean_col[:], rests, start=True, stop=True)
                        for h in range(RESTS):
                            ins = nc.tensor.matmul(chain_ps[rows, C_OUTER:C_OUTER + G],
                                                   rests[:, h:h + 1].to_broadcast([P, G]), mean_col[:],
                                                   start=h == 0, stop=h == RESTS - 1)
                    ins.then_inc(chain_pe, 1)
                    return
                pe.wait_ge(chain_dve, DVE_TOTAL * s + dve_needed(t))
                y_d, z_d = yz_all[:, 0, :], yz_all[:, 1, :]
                if t == NORM:
                    ins = nc.tensor.matmul(chain_ps[0:Q, C_NORM:C_NORM + 1], blocks[:, 0:PAIR, :].rearrange("p b g -> p (b g)"),
                                           col_all[:, 0:1], start=True, stop=True)
                elif t == NEXT_0:
                    ins = nc.tensor.matmul(chain_ps[0:Q, C_NEXT:C_NEXT + Q], y_d, z_d, start=True, stop=True)
                elif t < FOLD and (t - NEXT_0) % 2 == 1:
                    if t != FOLD - 2:
                        nc.tensor.matmul(chain_ps[0:Q, C_PRODUCT:C_PRODUCT + Q], z_d, y_d, start=True, stop=True)
                    ins = nc.tensor.matmul(chain_ps[0:Q, C_PRODUCT + Q:C_PRODUCT + 2 * Q], y_d, z_d, start=True, stop=True)
                elif t < FOLD:
                    if t != FOLD - 1:
                        nc.tensor.matmul(chain_ps[0:Q, C_NEXT:C_NEXT + Q], y_d, tu_all[:, 0, :], start=True, stop=True)
                    ins = nc.tensor.matmul(chain_ps[0:Q, C_NEXT + Q:C_NEXT + 2 * Q], z_d, tu_all[:, 1, :], start=True, stop=True)
                elif t == FOLD:
                    ins = nc.tensor.matmul(chain_ps[0:Q, C_PRODUCT:C_PRODUCT + G], z_d, w_t[:], start=True, stop=True)
                else:
                    for i in range(PAIR):
                        at = C_SPREAD + G * i
                        nc.tensor.matmul(chain_ps[:, at:at + G], pick[:, i, :, :].rearrange("p b g -> p (b g)"),
                                         folded[:, 0, :], start=True, stop=True)
                    ins = nc.tensor.matmul(chain_ps[:, C_OFFSET:C_OFFSET + PAIR],
                                           folded[:].rearrange("p b g -> p (b g)"), d_mask[:],
                                           start=True, stop=True)
                ins.then_inc(chain_pe, 1)

            def covariance(r, c, i, q):
                n = image(r, c, i)
                if q == 0:
                    pe.wait_ge(cov_read, n + 1)
                if plain(r, c):
                    pe.wait_ge(transposed, 2 * (IMAGE_PIECES * n + q) + 2)
                else:
                    pe.wait_ge(low_ready, split_piece(r, c, i, q) + PIECES + 1)
                for b in range(PIECE_BLOCKS):
                    if plain(r, c):
                        left = right = whole[q][:, 0, P * b:P * (b + 1)]
                    else:
                        both = parts[q][:, :, P * b:P * (b + 1)]
                        left, right = both[:, 0, :], both
                    ins = nc.tensor.matmul(cov_ps[:, i, 0:P if plain(r, c) else 2 * P], left, right, start=q == 0 and b == 0,
                                           stop=q == IMAGE_PIECES - 1 and b == PIECE_BLOCKS - 1)
                ins.then_inc(cov_done, 1)

            def output(r, c, i, q, part):
                if part == 0:
                    if i == 0 and q == 0:
                        pe.wait_ge(chain_dve, DVE_TOTAL * (PERIOD * r + c) + DVE_TOTAL)
                    pe.wait_ge(y_read, IMAGE_PIECES * image(r, c, i) + q + 1)
                h, o = q // PIECES, q % PIECES * PIECE
                a, z = ((BANK, PIECE), (0, BANK))[part]
                ins = nc.tensor.matmul(y_ps[:, q % 2, a:z], apply_w[:, c % 2, i, :, :].rearrange("p b g -> p (b g)"),
                                       xs[slot_of(c, i)][:, h, o + a:o + z], start=True, stop=True)
                if part == 1:
                    ins.then_inc(y_done, 1)

            def phase(r, c):
                for f, m, t, pair in places(r, c):
                    i, q = f // IMAGE_PIECES, f % IMAGE_PIECES
                    if m == 0 and exists(r, c):
                        covariance(r, c, i, q)
                    done = output_at(c, f)
                    if exists(r, done[0]):
                        output(r, *done, m)
                    if t is not None:
                        chain(r, pair, t)
                    ahead = later(c, i, 2)
                    if m == 1 and q == SHIFT_AT and exists(r, ahead[0]):
                        shift_of(r, *ahead)

            pe.wait_ge(shift_mat_ready, 1)
            for i in range(PAIR):
                shift_of(0, 0, i)
            pe.wait_ge(consts_ready, 1)
            phases(pe, phase)


def kernel(x, L0_conv_weight1, L0_conv_bias1):
    import numpy as np
    import concourse.bacc as bacc
    from concourse.bass_utils import run_bass_kernel_spmd

    nc = bacc.Bacc("TRN2", target_bir_lowering=False, num_devices=1)
    arrays = {"x": np.ascontiguousarray(x), "weight1": np.ascontiguousarray(L0_conv_weight1),
              "bias1": np.ascontiguousarray(L0_conv_bias1)}
    ins = [nc.dram_tensor(name, a.shape, mybir.dt.from_np(a.dtype), kind="ExternalInput").ap()
           for name, a in arrays.items()]
    out = nc.dram_tensor("y", arrays["x"].shape, FP32, kind="ExternalOutput").ap()
    whiten(nc, *ins, out)
    return run_bass_kernel_spmd(nc, [arrays], core_ids=[0]).results[0]["y"]
```

```python
from contextlib import ExitStack

import concourse.bass as bass
from concourse import mybir

FP32 = mybir.dt.float32
FP32R = mybir.dt.float32r
ALU = mybir.AluOpType
ACT = mybir.ActivationFunctionType
AX = mybir.AxisListType

IMAGES, CHANNELS, PIXELS = 32, 256, 48 * 48
G = 32
P = 128
BLOCKS = P // G
HALVES = CHANNELS // P
SAMPLES = CHANNELS // G * PIXELS
EPS = 1e-5
NEWTON = 10
PAIR = 2
PAIRS = IMAGES // PAIR
SLOTS = 8
PERIOD = SLOTS // PAIR
Q = PAIR * G
SHIFT_PIXELS = PIXELS // 2
PIECES = 3
PIECE = PIXELS // PIECES
IMAGE_PIECES = HALVES * PIECES
PIECE_BLOCKS = PIECE // P
ACT_HIGH = (2, 4)
SHIFT_AT = 1
CENTRE_PARTS = 2
RESTS = HALVES * CENTRE_PARTS
PLAIN = 2
BANK = 512

GATHER, NORM, NEXT_0 = 0, 1, 2
FOLD = NEXT_0 + 1 + 2 * (NEWTON - 1)
SPREAD = FOLD + 1
STEPS = SPREAD + 1
ASIDE = NEXT_0 + 8
EXTRA = [int(ASIDE <= t < ASIDE + 4) for t in range(STEPS)]
DVE_OPS = [m + e for m, e in zip([4, 5] + [1] * (STEPS - 3) + [2], EXTRA)]
DVE_TOTAL = sum(DVE_OPS)
PLACES = [1, 2] + list(range(4, STEPS + 2))
FLAT = PAIR * IMAGE_PIECES
STEP_AT = {place: t for t, place in enumerate(PLACES)}
assert PLACES[-1] == 2 * FLAT


def works(*places):
    return [[(w[0], *map(int, w[1:].split("."))) for w in place.split()] for place in places]


BULK = works("H0.5", "T1.0 T1.1", "", "T1.2", "H1.0", "T1.3 T1.4",
             "T1.5", "H1.1 T1.6", "T1.7", "H1.3 T1.8", "E0", "T1.9 T1.10",
             "T1.11 H1.5", "T2.0", "T2.1 H2.0", "T2.2", "T2.3", "T2.4 T2.5",
             "H2.1", "T2.6 T2.7", "H2.3", "T2.8 T2.9", "E1", "T2.10 T2.11")
BULK_PLAIN = works("", "T1.0", "T1.1", "", "T1.2", "T1.3 T1.4",
                   "T1.5", "T1.6", "T1.7", "T1.8", "T1.9 E0", "T1.10",
                   "T1.11 T2.0", "T2.1", "H2.0 T2.2", "T2.3", "H2.1 T2.4", "T2.5",
                   "T2.6", "T2.7", "H2.3 T2.8", "T2.9", "E1", "T2.10 T2.11")
HIGH_SCALAR = {4: (1, 2), 5: (1, 4), 8: (2, 2), 11: (2, 4)}
CENTRE_AT = (1, 2, 3, 4)
FILL_SCALAR = {(0, 0): [(2, "sum")], (0, 1): [(2, (0, 1))], (0, 2): [(2, (2, 3))], (0, 3): [(3, "sum")],
               (1, 0): [(3, (0,))], (1, 1): [(3, (1,))], (1, 2): [(3, (2,))], (1, 3): [(3, (3,))],
               (1, 4): [(4, "sum")], (1, 5): [(4, (0, 1))], (1, 6): [(4, (2,))], (1, 7): [(4, (3,)), (5, "sum")],
               (1, 10): [(5, (0, 1))], (1, 11): [(5, (2, 3))]}
FILL_SHIFT = {(0, 2): 1, (0, 7): 2, (1, 0): 3, (1, 5): 4, (1, 10): 5}


C_COV, C_REST, C_OUTER, C_NORM = 0, G, G + 1, 2 * G + 1
C_PRODUCT, C_NEXT, C_SPREAD, C_OFFSET = 0, 2 * Q, 2 * Q, 0


def dve_after(step):
    return sum(DVE_OPS[:step + 1])


def dve_needed(step):
    return dve_after(step - 1) - EXTRA[step - 1]


def whiten(nc, x, weight, bias, out):
    x_v = x.rearrange("n (h p) a b -> n p h (a b)", h=HALVES)
    out_v = out.rearrange("n (h p) a b -> n p h (a b)", h=HALVES)
    ctx = ExitStack()
    with ctx:
        def sb(name, shape, dt=FP32):
            return ctx.enter_context(nc.sbuf_tensor(name, shape, dt))

        def pb(name, shape):
            return ctx.enter_context(nc.psum_tensor(name, shape, FP32))

        def sem(name):
            return ctx.enter_context(nc.semaphore(name))

        xs = [sb(f"image{i}", [P, HALVES, PIXELS]) for i in range(SLOTS)]
        xt = [sb(f"transposed{i}", [P, PIECE]) for i in range(PIECES)]
        with ExitStack() as early:
            whole = [early.enter_context(nc.sbuf_tensor(f"whole{i}", [P, 2, PIECE], FP32)) for i in range(IMAGE_PIECES)]
        parts = [sb(f"parts{i}", [P, 2, PIECE], FP32R) for i in range(IMAGE_PIECES)]
        junk = sb("junk", [P, SHIFT_PIXELS], mybir.dt.bfloat16)
        eye = sb("eye", [P, P])
        eye_col = sb("eye_col", [P, G])
        mean_col = sb("mean_col", [P, G])
        shift_mat = sb("shift_mat", [P, P])
        blocks = sb("blocks", [P, BLOCKS, G])
        pick = sb("pick", [Q, PAIR, BLOCKS, G])
        eps_eye = sb("eps_eye", [Q, G])
        blocks2 = sb("blocks2", [Q, PAIR, G])
        eye15 = sb("eye15", [Q, 2, Q])
        w_nat = sb("w_nat", [P, G])
        w_t = sb("w_t", [P, G])
        b_col = sb("b_col", [P, 1])
        shift_sum = sb("shift_sum", [P, 2])
        shift = sb("shift", [P, 2])
        masked = sb("masked", [P, 2, BLOCKS, G])
        halved = sb("halved", [P, 2, BLOCKS // 2, G])
        halved_rest = sb("halved_rest", [P, RESTS // 2])
        stats = sb("stats", [P, 2, PAIR, 2 * G + 1 + RESTS])
        d_col = sb("d_col", [Q, 1])
        d_mask = sb("d_mask", [Q, PAIR])
        outer = sb("outer", [Q, G])
        cov = sb("cov", [Q, G])
        cov_sq = sb("cov_sq", [Q, G])
        col_all = sb("col", [P, 11])
        yz_all = sb("yz", [P, 2, Q])
        tu_all = sb("tu", [P, 2, Q])
        col, yz, tu = col_all[0:Q, :], yz_all[0:Q], tu_all[0:Q]
        folded = sb("folded", [Q, BLOCKS, G])
        apply_w = sb("apply_w", [P, 2, PAIR, BLOCKS, G])
        y_bias = sb("y_bias", [P, 2, PAIR])
        credits = sb("credits", [P, 24])
        ROW, ROOT, RECIP, TWICE, HALF_RN, HALF_ROOT, RECIP2, QUOTIENT, RSQ = (col[:, i:i + 1] for i in range(9))

        cov_ps = pb("cov_ps", [P, 2, BANK])
        y_ps = pb("y_ps", [P, 2, 2, BANK])
        chain_ps = pb("chain_ps", [P, BANK])
        shift_ps = pb("shift_ps", [P, BANK])

        consts_in = sem("consts_in")
        first_in = sem("first_in")
        loaded = [[sem(f"loaded{i}_{h}") for h in range(HALVES)] for i in range(SLOTS)]
        stored = [[sem(f"stored{i}_{h}") for h in range(HALVES)] for i in range(SLOTS)]
        eye_ready = sem("eye_ready")
        setup_pool = sem("setup_pool")
        setup_dve = sem("setup_dve")
        shift_mat_ready = sem("shift_mat_ready")
        consts_ready = sem("consts_ready")
        summed = sem("summed")
        shift_ready = sem("shift_ready")
        shift_copied = sem("shift_copied")
        centred = sem("centred")
        transposed = sem("transposed")
        high_dve = sem("high_dve")
        high_act = sem("high_act")
        low_ready = sem("low_ready")
        cov_done = sem("cov_done")
        cov_read = sem("cov_read")
        halved_ready = sem("halved_ready")
        stats_ready = sem("stats_ready")
        chain_pe = sem("chain_pe")
        chain_dve = sem("chain_dve")
        chain_act = sem("chain_act")
        y_done = sem("y_done")
        y_read = sem("y_read")

        block = ctx.enter_context(nc.Block())

        def exists(r, c):
            return not isinstance(r, int) or 0 <= c < PAIRS

        def image(r, c, i):
            return PAIR * PERIOD * r + PAIR * c + i

        def slot_of(c, i):
            return PAIR * (c % PERIOD) + i

        def later(c, i, d):
            return c + (i + d) // PAIR, (i + d) % PAIR

        def plain(r, c):
            return isinstance(r, int) and c < PLAIN

        def split_piece(r, c, i, q):
            return IMAGE_PIECES * (image(r, c, i) - PAIR * PLAIN) + q

        def places(r, c):
            for f in range(FLAT):
                for m in range(2):
                    if f == 0 and m == 0:
                        t, pair = STEP_AT[2 * FLAT], c - 2
                    else:
                        t, pair = STEP_AT.get(2 * f + m), c - 1
                    yield f, m, t if exists(r, pair) else None, pair

        def output_at(c, f):
            pair, flat = (c - 2, f - 1) if f else (c - 3, FLAT - 1)
            return pair, flat // IMAGE_PIECES, flat % IMAGE_PIECES

        def phases(eng, phase):
            steady = (PAIRS - 3) // PERIOD
            for c in range(3):
                phase(0, c)
            with eng.Fori(0, steady) as r:
                for c in range(3, 3 + PERIOD):
                    phase(r, c)
            for c in range(3 + PERIOD * steady, PAIRS + 3):
                phase(0, c)

        def evenly(r, c):
            return isinstance(r, int) and c >= PAIRS

        def by_piece(r, c, i):
            return isinstance(r, int) and (c, i) == (PAIRS - 1, PAIR - 1)

        @block.sync
        def _(sp):
            for n in range(SLOTS):
                for h in range(HALVES):
                    a = 0
                    if n == h == 0:
                        a = SHIFT_PIXELS
                        sp.dma_start(xs[n][:, h, 0:a], x_v[n, :, h, 0:a]).then_inc(first_in, 16)
                    sp.dma_start(xs[n][:, h, a:], x_v[n, :, h, a:]).then_inc(loaded[n][h], 16)
                if n == PAIR - 1:
                    for b in range(BLOCKS):
                        sp.dma_start(w_nat[G * b:G * (b + 1), :], weight[0]).then_inc(consts_in, 16)
                        sp.dma_start(b_col[G * b:G * (b + 1), :], bias[0]).then_inc(consts_in, 16)
            with sp.Fori(0, IMAGES // SLOTS - 1) as r:
                for n in range(SLOTS):
                    for h in range(HALVES):
                        sp.wait_ge(stored[n][h], 16 * r + 16)
                        src = x_v[bass.ds(SLOTS * r + SLOTS + n, 1), :, h, :].rearrange("o p s -> p (o s)")
                        sp.dma_start(xs[n][:, h, :], src).then_inc(loaded[n][h], 16)

        @block.gpsimd
        def _(pool):
            nc.gpsimd.memset(eye[:], 0.0).then_inc(setup_pool, 1)
            pool.wait_ge(setup_pool, 1)
            nc.gpsimd.affine_select(out=eye[:], in_=eye[:], compare_op=ALU.not_equal, fill=1.0, base=0,
                                    pattern=[[-1, P]], channel_multiplier=1).then_inc(eye_ready, 1)

            def low(m, q):
                if q in ACT_HIGH:
                    pool.wait_ge(high_act, len(ACT_HIGH) * m + ACT_HIGH.index(q) + 1)
                else:
                    rest = [p for p in range(IMAGE_PIECES) if p not in ACT_HIGH]
                    pool.wait_ge(high_dve, len(rest) * m + rest.index(q) + 1)
                nc.gpsimd.tensor_tensor(parts[q][:, 1, :], xt[q % PIECES][:], parts[q][:, 0, :].bitcast(FP32),
                                        ALU.subtract).then_inc(low_ready, 1)

            def add_blocks(n, c, i):
                pool.wait_ge(cov_read, n + 1 + 2)
                pool.wait_ge(stats_ready, 2 * n + 2)
                nc.gpsimd.tensor_tensor(halved[:], masked[:, :, 0:2], masked[:, :, 2:4], ALU.add).then_inc(halved_ready, 1)
                pool.wait_ge(centred, RESTS * n + RESTS)
                image_stats = stats[:, c % 2, i]
                rest = image_stats[:, 2 * G + 1:2 * G + 1 + RESTS]
                nc.gpsimd.tensor_tensor(halved_rest[:], rest[:, 0:2], rest[:, 2:4], ALU.add).then_inc(halved_ready, 1)
                pool.wait_ge(halved_ready, 2 * n + 2)
                nc.gpsimd.tensor_tensor(image_stats[:, 0:2 * G].rearrange("p (m g) -> p m g", m=2),
                                        halved[:, :, 0], halved[:, :, 1], ALU.add).then_inc(stats_ready, 1)
                nc.gpsimd.tensor_tensor(image_stats[:, 2 * G:2 * G + 1], halved_rest[:, 0:1], halved_rest[:, 1:2],
                                        ALU.add).then_inc(stats_ready, 1)

            unsplit = PAIR * PLAIN
            for n in range(unsplit - 1):
                add_blocks(n, n // PAIR, n % PAIR)
            with pool.Fori(0, (IMAGES - unsplit) // (2 * PAIR)) as r:
                for u in range(2 * PAIR):
                    for q in range(IMAGE_PIECES):
                        low(2 * PAIR * r + u, q)
                        if q == PIECES:
                            before = unsplit + u - 1
                            add_blocks(2 * PAIR * r + before, before // PAIR, before % PAIR)
            add_blocks(IMAGES - 1, PAIRS - 1, PAIR - 1)

        @block.scalar
        def _(act):
            def sum_shift(r, c, i):
                n = image(r, c, i)
                if isinstance(n, int) and n == 0:
                    act.wait_ge(first_in, 16)
                else:
                    act.wait_ge(loaded[slot_of(c, i)][0], 16 * (r + c // PERIOD) + 16)
                nc.scalar.activation(junk[:], xs[slot_of(c, i)][:, 0, 0:SHIFT_PIXELS], ACT.Identity,
                                     accum_out=shift_sum[:, i:i + 1]).then_inc(summed, 1)

            def centre(r, c, i, k):
                n = image(r, c, i)
                h, o = k // CENTRE_PARTS, k % CENTRE_PARTS * (PIXELS // CENTRE_PARTS)
                if k == 0:
                    act.wait_ge(shift_ready, n + 1)
                    nc.scalar.copy(shift[:, i:i + 1], shift_ps[:, 0:1]).then_inc(shift_copied, 1)
                    act.wait_ge(shift_copied, n + 1 + 1)
                part = xs[slot_of(c, i)][:, h, o:o + PIXELS // CENTRE_PARTS]
                if not (isinstance(n, int) and n == k == 0):
                    act.wait_ge(loaded[slot_of(c, i)][h], 16 * (r + c // PERIOD) + 16)
                nc.scalar.activation(part, part, ACT.Identity, bias=shift[:, i:i + 1],
                                     accum_out=stats[:, c % 2, i, 2 * G + 1 + k:2 * G + 2 + k]).then_inc(centred, 1)

            def high(r, c, i, q):
                act.wait_ge(transposed, 2 * (IMAGE_PIECES * image(r, c, i) + q) + 2)
                act.wait_ge(cov_done, IMAGE_PIECES * image(r, c, i) + q + 1)
                nc.scalar.copy(parts[q][:, 0, :], xt[q % PIECES][:]).then_inc(high_act, 1)

            def output(r, c, i, q, even):
                m = IMAGE_PIECES * image(r, c, i) + q
                h, o = q // PIECES, q % PIECES * PIECE
                if i == 0 and q == 0:
                    act.wait_ge(chain_dve, DVE_TOTAL * (PERIOD * r + c) + DVE_TOTAL)
                act.wait_ge(y_done, m + 1)
                slot = xs[slot_of(c, i)]
                if even:
                    src = y_ps[:, q % 2, :, 0:PIECE // 2]
                    dst = slot[:, h, o:o + PIECE].rearrange("p (t s) -> p t s", t=2)
                else:
                    src = y_ps[:, q % 2].rearrange("p t s -> p (t s)")[:, 0:PIECE]
                    dst = slot[:, h, o:o + PIECE]
                nc.scalar.activation(dst, src, ACT.Identity,
                                     bias=y_bias[:, c % 2, i:i + 1]).then_inc(y_read, 1)
                if by_piece(r, c, i):
                    act.wait_ge(y_read, m + 1 + 2)
                    act.dma_start(out_v[image(r, c, i), :, h, o:o + PIECE], slot[:, h, o:o + PIECE]).then_inc(
                        stored[slot_of(c, i)][h], 16)
                elif q % PIECES == PIECES - 1:
                    act.wait_ge(y_read, m + 1 + 2)
                    n = image(r, c, i)
                    dst = out_v[n, :, h, :] if isinstance(n, int) else out_v[bass.ds(n, 1), :, h, :].rearrange("o p s -> p (o s)")
                    act.dma_start(dst, slot[:, h, :]).then_inc(stored[slot_of(c, i)][h], 16)

            def root(r, c, half):
                s = PERIOD * r + c
                if half:
                    act.wait_ge(chain_dve, DVE_TOTAL * s + dve_after(NORM))
                    nc.scalar.activation(HALF_ROOT, HALF_RN, ACT.Sqrt, scale=0.5).then_inc(chain_act, 1)
                else:
                    act.wait_ge(chain_pe, STEPS * s + NORM + 1)
                    nc.scalar.activation(ROOT, chain_ps[0:Q, C_NORM:C_NORM + 1], ACT.Sqrt).then_inc(chain_act, 1)

            def phase(r, c):
                for f in range(FLAT):
                    i, q = f // IMAGE_PIECES, f % IMAGE_PIECES
                    if f in (1, 2) and exists(r, c - 1):
                        root(r, c - 1, f == 2)
                    done = output_at(c, f)
                    if exists(r, done[0]):
                        output(r, *done, evenly(r, c))
                    ahead = later(c, i, 2)
                    if f in HIGH_SCALAR:
                        n, piece = HIGH_SCALAR[f]
                        target = later(c, 0, n)
                        if exists(r, target[0]) and not plain(r, target[0]):
                            high(r, *target, piece)
                    if plain(r, c):
                        for n, what in FILL_SCALAR.get((c, f), []):
                            if what == "sum":
                                sum_shift(0, n // PAIR, n % PAIR)
                            else:
                                for k in what:
                                    centre(0, n // PAIR, n % PAIR, k)
                    elif exists(r, ahead[0]):
                        if q == 0:
                            sum_shift(r, *ahead)
                        for k, at in enumerate(CENTRE_AT):
                            if q == at:
                                centre(r, *ahead, k)

            for i in range(PAIR):
                sum_shift(0, 0, i)
                for k in range(RESTS):
                    centre(0, 0, i, k)
            phases(act, phase)
            for n in range(SLOTS):
                for h in range(HALVES):
                    stores = IMAGES // SLOTS + (PIECES - 1 if n == SLOTS - 1 else 0)
                    act.wait_ge(stored[n][h], 16 * stores)

        @block.vector
        def _(dve):
            done = [0]

            def then(ins):
                done[0] += 1
                ins.then_inc(setup_dve, 1)
                dve.wait_ge(setup_dve, done[0])

            dve.wait_ge(eye_ready, 1)
            for b in range(BLOCKS):
                rows = slice(G * b, G * (b + 1))
                then(nc.vector.tensor_copy(eye_col[rows, :], eye[rows, rows]))
            for b in range(BLOCKS):
                then(nc.vector.tensor_scalar(shift_mat[:, G * b:G * (b + 1)], eye_col[:],
                                             -1.0 / (BLOCKS * SHIFT_PIXELS), None, ALU.mult))
            ahead = ([shift_copied, shift_mat_ready, stats_ready, stats_ready] + [cov_read, y_read] * 2 + [cov_done] * IMAGE_PIECES
                     + [low_ready] * PIECES)
            for i, free in enumerate(ahead):
                nc.vector.memset(credits[:, i:i + 1], 0.0).then_inc(free, 1)
            for padded in (col_all, yz_all, blocks, masked):
                then(nc.vector.memset(padded[:], 0.0))
            then(nc.vector.memset(tu_all[:], 0.0))
            for b in range(BLOCKS):
                then(nc.vector.memset(blocks[G * b:G * (b + 1), b, :], 1.0))

            def transpose(r, c, i, k):
                q, part = k // 2, k % 2
                h, o = q // PIECES, q % PIECES
                a = PIECE // 2 * part
                z = a + PIECE // 2
                of_half = PIECE * o + a
                if of_half % (PIXELS // CENTRE_PARTS) == 0:
                    dve.wait_ge(centred, RESTS * image(r, c, i) + CENTRE_PARTS * h + of_half // (PIXELS // CENTRE_PARTS) + 1)
                if plain(r, c):
                    if part == 0:
                        dve.wait_ge(cov_done, IMAGE_PIECES * image(r, c, i) + q + 1)
                    dst = whole[q][:, 0, a:z]
                else:
                    if part == 0:
                        dve.wait_ge(low_ready, split_piece(r, c, i, q) + 1)
                    dst = xt[o][:, a:z]
                nc.vector.transpose(dst, xs[slot_of(c, i)][:, h, of_half:of_half + PIECE // 2]).then_inc(transposed, 1)

            def high(r, c, i, q):
                m = IMAGE_PIECES * image(r, c, i) + q
                dve.wait_ge(transposed, 2 * m + 2)
                dve.wait_ge(cov_done, m + 1)
                nc.vector.tensor_copy(parts[q][:, 0, :], xt[q % PIECES][:]).then_inc(high_dve, 1)

            def covariance_out(r, c, i):
                n = image(r, c, i)
                dve.wait_ge(cov_done, IMAGE_PIECES * (n + 1) + IMAGE_PIECES)
                dve.wait_ge(stats_ready, 2 * n + 2)
                kinds = 1 if plain(r, c) else 2
                nc.vector.tensor_tensor(masked[:, 0:kinds],
                                        cov_ps[:, i, 0:kinds * P].rearrange("p (m b g) -> p m b g", m=kinds, b=BLOCKS),
                                        blocks[:].unsqueeze(1).to_broadcast([P, kinds, BLOCKS, G]), ALU.mult).then_inc(cov_read, 1)

            def diagonal(dst, src, n, rows, count):
                return nc.vector.tensor_tensor(
                    dst, src.unsqueeze(2).to_broadcast([rows, n, count, G]),
                    blocks[0:rows, 0:count, :].unsqueeze(1).to_broadcast([rows, n, count, G]), ALU.mult)

            def chain(r, c, t):
                s = PERIOD * r + c
                at = [dve_after(t - 1) if t else 0]
                dve.wait_ge(chain_pe, STEPS * s + t + 1)

                def link(ins):
                    at[0] += 1
                    ins.then_inc(chain_dve, 1)
                    dve.wait_ge(chain_dve, DVE_TOTAL * s + at[0])

                product = chain_ps[0:Q, C_PRODUCT:C_PRODUCT + 2 * Q].rearrange("p (m g) -> p m g", m=2)
                following = chain_ps[0:Q, C_NEXT:C_NEXT + 2 * Q].rearrange("p (m g) -> p m g", m=2)
                if t == GATHER:
                    link(nc.vector.tensor_copy(d_col[:], chain_ps[0:Q, C_REST:C_REST + 1]))
                    link(nc.vector.scalar_tensor_tensor(out=outer[:], in0=chain_ps[0:Q, C_OUTER:C_OUTER + G],
                                                        scalar=d_col[:, 0:1], in1=eps_eye[:],
                                                        op0=ALU.mult, op1=ALU.subtract))
                    link(nc.vector.scalar_tensor_tensor(out=cov[:], in0=chain_ps[0:Q, C_COV:C_COV + G], scalar=1.0,
                                                        in1=outer[:], op0=ALU.mult, op1=ALU.subtract))
                    link(nc.vector.scalar_tensor_tensor(out=cov_sq[:], in0=cov[:], scalar=1.0, in1=cov[:],
                                                        op0=ALU.mult, op1=ALU.mult, accum_out=ROW))
                elif t == NORM:
                    dve.wait_ge(chain_act, 2 * s + 1)
                    link(nc.vector.reciprocal(RECIP, ROOT))
                    link(nc.vector.scalar_tensor_tensor(out=TWICE, in0=chain_ps[0:Q, C_NORM:C_NORM + 1], scalar=RECIP,
                                                        in1=ROOT, op0=ALU.mult, op1=ALU.add))
                    link(nc.vector.reciprocal(HALF_RN, TWICE))
                    link(nc.vector.scalar_tensor_tensor(
                        out=yz[:, 0, :].rearrange("p (b g) -> p b g", b=PAIR),
                        in0=cov[:].unsqueeze(1).to_broadcast([Q, PAIR, G]), scalar=HALF_RN, in1=blocks2[:],
                        op0=ALU.mult, op1=ALU.mult))
                    link(nc.vector.scalar_tensor_tensor(
                        out=yz[:, 1, :], in0=yz[:, 0, :], scalar=-0.5, in1=eye15[:, 0, :], op0=ALU.mult, op1=ALU.add))
                elif t == NEXT_0:
                    link(nc.vector.tensor_copy(yz[:, 0, :], following[:, 0, :]))
                elif t < FOLD and (t - NEXT_0) % 2 == 1:
                    first = 1 if t == FOLD - 2 else 0
                    link(nc.vector.scalar_tensor_tensor(out=tu[:, first:2], in0=product[:, first:2], scalar=-0.5,
                                                        in1=eye15[:, first:2], op0=ALU.mult, op1=ALU.add))
                elif t < FOLD:
                    first = 1 if t == FOLD - 1 else 0
                    link(nc.vector.tensor_copy(yz[:, first:2], following[:, first:2]))
                elif t == FOLD:
                    link(nc.vector.tensor_scalar(
                        folded[:], chain_ps[0:Q, C_PRODUCT:C_PRODUCT + G].unsqueeze(1).to_broadcast([Q, BLOCKS, G]),
                        RSQ, None, ALU.mult))
                else:
                    if exists(r, c - 2):
                        dve.wait_ge(y_read, IMAGE_PIECES * image(r, c - 1, 0) + 2)
                    spread = chain_ps[:, C_SPREAD:C_SPREAD + PAIR * G].rearrange("p (i g) -> p i g", i=PAIR)
                    link(diagonal(apply_w[:, c % 2], spread, PAIR, P, BLOCKS))
                    link(nc.vector.tensor_scalar(y_bias[:, c % 2, :], chain_ps[:, C_OFFSET:C_OFFSET + PAIR], -1.0,
                                                 b_col[:, 0:1], ALU.mult, ALU.add))

                if t == ASIDE:
                    link(nc.vector.tensor_scalar(d_mask[:], blocks[0:Q, 0:PAIR, 0], d_col[:, 0:1], None, ALU.mult))
                elif t == ASIDE + 1:
                    dve.wait_ge(chain_act, 2 * s + 2)
                    link(nc.vector.reciprocal(RECIP2, HALF_ROOT))
                elif t == ASIDE + 2:
                    link(nc.vector.tensor_scalar(QUOTIENT, RECIP2, HALF_RN, 0.5, ALU.mult, ALU.mult))
                elif t == ASIDE + 3:
                    link(nc.vector.tensor_tensor(RSQ, QUOTIENT, HALF_ROOT, ALU.add))

            def phase(r, c):
                for f, m, t, pair in places(r, c):
                    if t is not None:
                        chain(r, pair, t)
                    for kind, n, *what in (BULK_PLAIN if plain(r, c) else BULK)[2 * f + m]:
                        target = later(c, 0, n)
                        if not exists(r, target[0]):
                            continue
                        if kind == "E":
                            covariance_out(r, *target)
                        elif kind == "T":
                            transpose(r, *target, *what)
                        elif not plain(r, target[0]):
                            high(r, *target, *what)

            for k in range(2 * IMAGE_PIECES):
                transpose(0, 0, 0, k)
            then(nc.vector.tensor_scalar(mean_col[:], eye_col[:], 1.0 / SAMPLES, None, ALU.mult))
            then(nc.vector.tensor_scalar(eps_eye[:], eye_col[0:Q, :], EPS, None, ALU.mult))
            for b in range(BLOCKS):
                for i in range(PAIR):
                    then(nc.vector.tensor_copy(pick[:, i, b, :], eye[0:Q, G * i:G * (i + 1)]))
            then(nc.vector.tensor_scalar(blocks2[:], blocks[0:Q, 0:PAIR, :], 2.0, None, ALU.mult))
            for m in range(2):
                then(nc.vector.tensor_scalar(eye15[:, m, :], eye[0:Q, 0:Q], 1.5, None, ALU.mult))
            dve.wait_ge(consts_in, 16 * 2 * BLOCKS)
            then(nc.vector.transpose(w_t[:], w_nat[:]))
            nc.vector.memset(credits[:, len(ahead):len(ahead) + 1], 0.0).then_inc(consts_ready, 1)
            phases(dve, phase)

        @block.tensor
        def _(pe):
            def shift_of(r, c, i):
                n = image(r, c, i)
                pe.wait_ge(summed, n + 1)
                pe.wait_ge(shift_copied, n + 1)
                nc.tensor.matmul(shift_ps[:, 0:1], shift_mat[:], shift_sum[:, i:i + 1],
                                 start=True, stop=True).then_inc(shift_ready, 1)

            def chain(r, c, t):
                s = PERIOD * r + c
                if t == GATHER:
                    pe.wait_ge(stats_ready, 2 * (PAIR * s + PAIR) + 2)
                    if exists(r, c - 1):
                        pe.wait_ge(chain_dve, DVE_TOTAL * s)
                    for i in range(PAIR):
                        rows = slice(G * i, G * (i + 1))
                        squares, crossed, rest = (stats[:, c % 2, i, G * m:min(G * (m + 1), 2 * G + 1)] for m in range(3))
                        sums = chain_ps[rows, C_COV:C_COV + G]
                        nc.tensor.matmul(sums, mean_col[:], squares, start=True, stop=plain(r, c))
                        if not plain(r, c):
                            nc.tensor.matmul(sums, mean_col[:], crossed, start=False, stop=False)
                            nc.tensor.matmul(sums, crossed, mean_col[:], start=False, stop=True)
                        nc.tensor.matmul(chain_ps[rows, C_REST:C_REST + 1], mean_col[:], rest, start=True, stop=True)
                        ins = nc.tensor.matmul(chain_ps[rows, C_OUTER:C_OUTER + G], rest.to_broadcast([P, G]), mean_col[:],
                                               start=True, stop=True)
                    ins.then_inc(chain_pe, 1)
                    return
                pe.wait_ge(chain_dve, DVE_TOTAL * s + dve_needed(t))
                y_d, z_d = yz_all[:, 0, :], yz_all[:, 1, :]
                if t == NORM:
                    ins = nc.tensor.matmul(chain_ps[0:Q, C_NORM:C_NORM + 1], blocks[:, 0:PAIR, :].rearrange("p b g -> p (b g)"),
                                           col_all[:, 0:1], start=True, stop=True)
                elif t == NEXT_0:
                    ins = nc.tensor.matmul(chain_ps[0:Q, C_NEXT:C_NEXT + Q], y_d, z_d, start=True, stop=True)
                elif t < FOLD and (t - NEXT_0) % 2 == 1:
                    if t != FOLD - 2:
                        nc.tensor.matmul(chain_ps[0:Q, C_PRODUCT:C_PRODUCT + Q], z_d, y_d, start=True, stop=True)
                    ins = nc.tensor.matmul(chain_ps[0:Q, C_PRODUCT + Q:C_PRODUCT + 2 * Q], y_d, z_d, start=True, stop=True)
                elif t < FOLD:
                    if t != FOLD - 1:
                        nc.tensor.matmul(chain_ps[0:Q, C_NEXT:C_NEXT + Q], y_d, tu_all[:, 0, :], start=True, stop=True)
                    ins = nc.tensor.matmul(chain_ps[0:Q, C_NEXT + Q:C_NEXT + 2 * Q], z_d, tu_all[:, 1, :], start=True, stop=True)
                elif t == FOLD:
                    ins = nc.tensor.matmul(chain_ps[0:Q, C_PRODUCT:C_PRODUCT + G], z_d, w_t[:], start=True, stop=True)
                else:
                    for i in range(PAIR):
                        at = C_SPREAD + G * i
                        nc.tensor.matmul(chain_ps[:, at:at + G], pick[:, i, :, :].rearrange("p b g -> p (b g)"),
                                         folded[:, 0, :], start=True, stop=True)
                    ins = nc.tensor.matmul(chain_ps[:, C_OFFSET:C_OFFSET + PAIR],
                                           folded[:].rearrange("p b g -> p (b g)"), d_mask[:],
                                           start=True, stop=True)
                ins.then_inc(chain_pe, 1)

            def covariance(r, c, i, q, blocks_of_piece):
                n = image(r, c, i)
                if q == 0 and blocks_of_piece[0] == 0:
                    pe.wait_ge(cov_read, n + 1)
                if plain(r, c):
                    pe.wait_ge(transposed, 2 * (IMAGE_PIECES * n + q) + 1 + blocks_of_piece[0] // (PIECE_BLOCKS // 2))
                else:
                    pe.wait_ge(low_ready, split_piece(r, c, i, q) + PIECES + 1)
                for b in blocks_of_piece:
                    if plain(r, c):
                        left = right = whole[q][:, 0, P * b:P * (b + 1)]
                    else:
                        both = parts[q][:, :, P * b:P * (b + 1)]
                        left, right = both[:, 0, :], both
                    ins = nc.tensor.matmul(cov_ps[:, i, 0:P if plain(r, c) else 2 * P], left, right, start=q == 0 and b == 0,
                                           stop=q == IMAGE_PIECES - 1 and b == PIECE_BLOCKS - 1)
                if b == PIECE_BLOCKS - 1:
                    ins.then_inc(cov_done, 1)

            def output(r, c, i, q, part, even):
                if part == 0:
                    if i == 0 and q == 0:
                        pe.wait_ge(chain_dve, DVE_TOTAL * (PERIOD * r + c) + DVE_TOTAL)
                    pe.wait_ge(y_read, IMAGE_PIECES * image(r, c, i) + q + 1)
                h, o = q // PIECES, q % PIECES * PIECE
                bank = 1 - part
                a, z = BANK * bank, min(BANK * (bank + 1), PIECE)
                if even:
                    a, z = PIECE // 2 * bank, PIECE // 2 * (bank + 1)
                ins = nc.tensor.matmul(y_ps[:, q % 2, bank, 0:z - a], apply_w[:, c % 2, i, :, :].rearrange("p b g -> p (b g)"),
                                       xs[slot_of(c, i)][:, h, o + a:o + z], start=True, stop=True)
                if part == 1:
                    ins.then_inc(y_done, 1)

            def phase(r, c):
                for f, m, t, pair in places(r, c):
                    i, q = f // IMAGE_PIECES, f % IMAGE_PIECES
                    if plain(r, c):
                        covariance(r, c, i, q, range(PIECE_BLOCKS // 2 * m, PIECE_BLOCKS // 2 * (m + 1)))
                        if m == 0 and (c, f) in FILL_SHIFT:
                            shift_of(0, FILL_SHIFT[c, f] // PAIR, FILL_SHIFT[c, f] % PAIR)
                    elif m == 0 and exists(r, c):
                        covariance(r, c, i, q, range(PIECE_BLOCKS))
                    done = output_at(c, f)
                    if exists(r, done[0]):
                        output(r, *done, m, evenly(r, c))
                    if (c, f, m) == (1, 0, 0):
                        pe.wait_ge(consts_ready, 1)
                    if t is not None:
                        chain(r, pair, t)
                    ahead = later(c, i, 2)
                    if m == 1 and q == SHIFT_AT and exists(r, ahead[0]) and not plain(r, c):
                        shift_of(r, *ahead)

            pe.wait_ge(shift_mat_ready, 1)
            shift_of(0, 0, 0)
            phases(pe, phase)


def kernel(x, L0_conv_weight1, L0_conv_bias1):
    import numpy as np
    import concourse.bacc as bacc
    from concourse.bass_utils import run_bass_kernel_spmd

    nc = bacc.Bacc("TRN2", target_bir_lowering=False, num_devices=1)
    arrays = {"x": np.ascontiguousarray(x), "weight1": np.ascontiguousarray(L0_conv_weight1),
              "bias1": np.ascontiguousarray(L0_conv_bias1)}
    ins = [nc.dram_tensor(name, a.shape, mybir.dt.from_np(a.dtype), kind="ExternalInput").ap()
           for name, a in arrays.items()]
    out = nc.dram_tensor("y", arrays["x"].shape, FP32, kind="ExternalOutput").ap()
    whiten(nc, *ins, out)
    return run_bass_kernel_spmd(nc, [arrays], core_ids=[0]).results[0]["y"]
```
